# Optimizing a Trainium2 kernel written in Bass

```python
import numpy as np
import jax
import jax.numpy as jnp

def _softmax(x, axis=-1):
    return jax.nn.softmax(x, axis=axis)

def _gelu(x):
    return jax.nn.gelu(x, approximate=True)

def _silu(x):
    return jax.nn.silu(x)

def _sigmoid(x):
    return jax.nn.sigmoid(x)

def _layernorm(x, axis=-1, eps=1e-05):
    m = jnp.mean(x, axis=axis, keepdims=True)
    v = jnp.var(x, axis=axis, keepdims=True)
    return (x - m) / jnp.sqrt(v + eps)

def _scatter_add(tgt, idx, src, axis=0):
    return tgt.at[idx].add(src)

def _segment_sum(src, seg, n):
    return jax.ops.segment_sum(src, seg, n)
kernel_name = 'mk_cond_resid_d2_seqx_r4_bbf4a2'

def setup_inputs(seed: int=0):
    np.random.seed(seed)
    _w = jnp.asarray

    def _rec_inputs():
        import jax
        import jax.numpy as jnp
        _rk = jax.random.key(seed)
        x = 7.22e-05 + 1 * jax.random.normal(jax.random.fold_in(_rk, 1), (4, 512, 256), jnp.float32)
        _lenS = 512 - jax.random.randint(jax.random.fold_in(_rk, 7), (4,), 0, max(1, 512 // 4) + 1, jnp.int32)
        _lenS2 = 512 - jax.random.randint(jax.random.fold_in(_rk, 8), (4,), 0, max(1, 512 // 4) + 1, jnp.int32)
        cond_8 = jax.random.uniform(jax.random.fold_in(_rk, 11), (4, 8), jnp.float32, 0.0, 0.999837)
        return (x, cond_8)
    x, cond_8 = _rec_inputs()

    def _L0_cond_setup():
        import jax, jax.numpy as jnp
        import numpy as np
        key = jax.random.key(seed)
        k1, k2, k3, k4, k5 = jax.random.split(key, 5)
        B, N, T, O, G = (32, 64, 256, 256, 8)
        x = jax.random.normal(k1, (B, N, T), dtype=jnp.float32)
        y = jax.random.uniform(k2, (B, G), dtype=jnp.float32)
        weight = jax.random.normal(k3, (G, O, T), dtype=jnp.float32) * (1.0 / np.sqrt(T))
        mask = jax.random.uniform(k4, (O, T), dtype=jnp.float32)
        bias = jax.random.normal(k5, (O,), dtype=jnp.float32)
        return {'x': x, 'y': y, 'weight': weight, 'mask': mask, 'bias': bias}
    _L0_cond_all = _L0_cond_setup()
    _L0_cond_in = {k: v for k, v in _L0_cond_all.items() if k in ('weight', 'mask', 'bias')}
    del _L0_cond_all

    def _L1_cond_setup():
        import jax, jax.numpy as jnp
        import numpy as np
        TOP_K = 2
        NUM_MOE_LAYERS = 12

        def _gemma_mlp(x, gate_w, up_w, down_w):
            g = jnp.einsum('bsh,hi->bsi', x, gate_w)
            u = jnp.einsum('bsh,hi->bsi', x, up_w)
            return jnp.einsum('bsi,ih->bsh', jax.nn.gelu(g, approximate=True) * u, down_w)
        key = jax.random.key(seed)
        ks = jax.random.split(key, 8)
        B, S, H, I, E = (32, 64, 256, 1024, 8)
        std = 0.02
        return {'x': jax.random.normal(ks[0], (B, S, H), jnp.float32), 'router_logits': jax.random.normal(ks[1], (B, E), jnp.float32), 'skill_gate': jax.random.normal(ks[2], (E, H, I), jnp.float32) * std, 'skill_up': jax.random.normal(ks[3], (E, H, I), jnp.float32) * std, 'skill_down': jax.random.normal(ks[4], (E, I, H), jnp.float32) * std, 'shared_gate': jax.random.normal(ks[5], (H, I), jnp.float32) * std, 'shared_up': jax.random.normal(ks[6], (H, I), jnp.float32) * std, 'shared_down': jax.random.normal(ks[7], (I, H), jnp.float32) * std}
    _L1_cond_all = _L1_cond_setup()
    _L1_cond_in = {k: v for k, v in _L1_cond_all.items() if k in ('skill_gate', 'skill_up', 'skill_down', 'shared_gate', 'shared_up', 'shared_down')}
    del _L1_cond_all
    return {'x': x, 'cond_8': cond_8, 'L0_cond_weight': _L0_cond_in['weight'], 'L0_cond_mask': _L0_cond_in['mask'], 'L0_cond_bias': _L0_cond_in['bias'], 'L1_cond_skill_gate': _L1_cond_in['skill_gate'], 'L1_cond_skill_up': _L1_cond_in['skill_up'], 'L1_cond_skill_down': _L1_cond_in['skill_down'], 'L1_cond_shared_gate': _L1_cond_in['shared_gate'], 'L1_cond_shared_up': _L1_cond_in['shared_up'], 'L1_cond_shared_down': _L1_cond_in['shared_down']}

def reference(x, cond_8, L0_cond_weight, L0_cond_mask, L0_cond_bias, L1_cond_skill_gate, L1_cond_skill_up, L1_cond_skill_down, L1_cond_shared_gate, L1_cond_shared_up, L1_cond_shared_down):
    import jax
    import jax.numpy as jnp

    def _L0_cond_ref(x, y, weight, mask, bias):
        import jax, jax.numpy as jnp
        import numpy as np
        masked_w = weight * mask[None, :, :]
        w_bot = jnp.einsum('bg,got->bot', y, masked_w)
        return jnp.einsum('bnt,bot->bno', x, w_bot) + bias

    def _L1_cond_ref(x, router_logits, skill_gate, skill_up, skill_down, shared_gate, shared_up, shared_down):
        import jax, jax.numpy as jnp
        import numpy as np
        TOP_K = 2
        NUM_MOE_LAYERS = 12

        def _gemma_mlp(x, gate_w, up_w, down_w):
            g = jnp.einsum('bsh,hi->bsi', x, gate_w)
            u = jnp.einsum('bsh,hi->bsi', x, up_w)
            return jnp.einsum('bsi,ih->bsh', jax.nn.gelu(g, approximate=True) * u, down_w)
        B = x.shape[0]
        E = skill_gate.shape[0]
        rw = jax.nn.softmax(router_logits.astype(jnp.float32), axis=-1)
        w, sel = jax.lax.top_k(rw, TOP_K)
        w = w / w.sum(axis=-1, keepdims=True)
        w = w.astype(x.dtype)
        scale = 1.0 / NUM_MOE_LAYERS
        w = scale * w + (1.0 - scale) * jax.lax.stop_gradient(w)
        dense_w = jnp.zeros((B, E), x.dtype).at[jnp.arange(B)[:, None], sel].add(w)

        def step(acc, params):
            g, u, d, we = params
            return (acc + we[:, None, None] * _gemma_mlp(x, g, u, d), None)
        out, _ = jax.lax.scan(step, jnp.zeros_like(x), (skill_gate, skill_up, skill_down, dense_w.T))
        out = out + _gemma_mlp(x, shared_gate, shared_up, shared_down)
        return out
    x = x + _L0_cond_ref(x, cond_8, L0_cond_weight, L0_cond_mask, L0_cond_bias)
    x = x + _L1_cond_ref(x, cond_8, L1_cond_skill_gate, L1_cond_skill_up, L1_cond_skill_down, L1_cond_shared_gate, L1_cond_shared_up, L1_cond_shared_down)
    return x

_drawn_inputs = setup_inputs


def setup_inputs(seed=0):
    import zlib

    import numpy as np

    out = dict(_drawn_inputs(seed))
    spreads = {}
    factors = {}
    for name, (base, spread) in spreads.items():
        noise = np.random.default_rng([zlib.crc32(name.encode()), seed]).standard_normal(out[name].shape)
        drawn = base * np.exp(spread * noise) if base else spread * noise
        out[name] = jnp.asarray(drawn.astype(out[name].dtype))
    for name, factor in factors.items():
        out[name] = (out[name] * factor).astype(out[name].dtype)
    return out
```

```python
from contextlib import ExitStack

import concourse.bass as bass
from concourse import mybir

P = 128
F32 = mybir.dt.float32
F32R = mybir.dt.float32r
U32 = mybir.dt.uint32
ALU = mybir.AluOpType
ACT = mybir.ActivationFunctionType
AX_X = mybir.AxisListType.X

TOP_K = 2
SCALE = 1.0 / 12
LAG = 2
RAW_SLOTS = 8
RING = 8
H_SLOTS = LAG + 1
SPLIT_LEAD = 4
L0_STEP = 13


def build(nc, xT, cond, l0_w, l0_mask, l0_bias, experts, shared, outT):
    B, _, HH, T = xT.shape
    G = l0_w.shape[0]
    E, CHUNKS, _, WC = experts.shape
    D = HH * P
    L0C = HH * D
    GATE, UP, DOWN = 0, D, 2 * D
    STEPS = (1 + TOP_K) * CHUNKS
    ECH = TOP_K * CHUNKS

    ROUTED_IDX = 2 * B
    ROUTED_SHIFTED = ROUTED_IDX + 1
    ROUTED_WEIGHTS = ROUTED_SHIFTED + 8

    with ExitStack() as ctx:
        def sb(name, shape, dt=F32):
            return ctx.enter_context(nc.sbuf_tensor(name, shape, dt))

        def psum(name, shape):
            return ctx.enter_context(nc.psum_tensor(name, shape, F32))

        def sem(name):
            return ctx.enter_context(nc.semaphore(name))

        cond_all = sb("cond_all", [P, B, E])
        top = sb("top", [P, B, 8])
        top_idx = sb("top_idx", [P, B, 8], U32)
        shifted = sb("shifted", [P, B, 8])
        exps = sb("exps", [P, B, 8])
        exp_sum = sb("exp_sum", [P, B])
        exp_rsum = sb("exp_rsum", [P, B])
        probs = sb("probs", [P, B, 8])
        pair_sum = sb("pair_sum", [P, B])
        pair_rsum = sb("pair_rsum", [P, B])
        pair = sb("pair", [P, B, TOP_K])
        pair_rest = sb("pair_rest", [P, B, TOP_K])
        route_w = sb("route_w", [P, B * TOP_K])
        cond_cur = sb("cond_cur", [P, G])
        route_cur = sb("route_cur", [P, TOP_K])
        l0_raw = sb("l0_raw", [P, G, L0C])
        mask = sb("mask", [P, L0C])
        bias = sb("bias", [P, HH])
        l0_acc = sb("l0_acc", [P, L0C])
        l0_cw = sb("l0_cw", [P, L0C])
        l0_hi = sb("l0_hi", [P, L0C], F32R)
        l0_lo = sb("l0_lo", [P, L0C], F32R)
        x_in = sb("x_in", [P, HH, T])
        x_hi = sb("x_hi", [P, HH, T], F32R)
        x_lo = sb("x_lo", [P, HH, T], F32R)
        x1 = sb("x1", [P, 2 * HH * T])
        x1_hi = sb("x1_hi", [P, 2 * HH * T], F32R)
        x1_lo = sb("x1_lo", [P, 2 * HH * T], F32R)
        raw = sb("raw", [P, RAW_SLOTS, WC])
        sh_hi = sb("sh_hi", [P, CHUNKS, WC], F32R)
        sh_lo = sb("sh_lo", [P, CHUNKS, WC], F32R)
        ex_hi = sb("ex_hi", [P, RING, WC], F32R)
        ex_lo = sb("ex_lo", [P, RING, WC], F32R)
        gelu = sb("gelu", [P, 2, T])
        h = sb("h", [P, 2, T])
        h_hi = sb("h_hi", [P, H_SLOTS, T], F32R)
        h_lo = sb("h_lo", [P, H_SLOTS, T], F32R)
        out_sb = sb("out_sb", [P, HH, T])

        g_ps = psum("g_ps", [P, 2, T])
        u_ps = psum("u_ps", [P, 2, T])
        o_ps = psum("o_ps", [P, HH, T])
        l0_ps = psum("l0_ps", [P, HH, T])

        cond_in = sem("cond_in")
        l0_in = [sem(f"l0_in{g}") for g in range(G // 2)]
        mask_in = sem("mask_in")
        bias_in = sem("bias_in")
        x_loaded = sem("x_loaded")
        raw_in = [sem(f"raw_in{i}") for i in range(RAW_SLOTS)]
        routed = sem("routed")
        exp_done = sem("exp_done")
        cond_picked = sem("cond_picked")
        route_picked = sem("route_picked")
        combined = sem("combined")
        masked = sem("masked")
        l0_hi_done = sem("l0_hi_done")
        l0_lo_done = sem("l0_lo_done")
        x_hi_done = sem("x_hi_done")
        x_lo_done = sem("x_lo_done")
        l0_done = sem("l0_done")
        x1_done = sem("x1_done")
        x1_hi_done = sem("x1_hi_done")
        x1_lo_done = sem("x1_lo_done")
        w_hi_done = sem("w_hi_done")
        w_lo_done = sem("w_lo_done")
        g_done = sem("g_done")
        u_done = sem("u_done")
        gelu_done = sem("gelu_done")
        h_done = sem("h_done")
        h_hi_done = sem("h_hi_done")
        h_lo_done = sem("h_lo_done")
        down_done = sem("down_done")
        sum0_done = sem("sum0_done")
        out_done = sem("out_done")
        stored = sem("stored")

        def x1_at(t, b, hh):
            at = (b % 2) * (HH * T) + hh * T
            return t[:, bass.ds(at, T)]

        block = ctx.enter_context(nc.Block())

        @block.sync
        def _(sp):
            def load_x(b):
                if not isinstance(b, int):
                    sp.wait_ge(x1_done, HH * b)
                sp.dma_start(x_in[:], xT[bass.ds(b, 1)].rearrange("a p h t -> (a p) h t")).then_inc(x_loaded, 16)

            def load_expert(b, j, e):
                sp.wait_ge(w_lo_done, ECH * b + CHUNKS + j - RAW_SLOTS + 1)
                src = experts[bass.ds(e, 1), j % CHUNKS].rearrange("a p w -> (a p) w")
                sp.dma_start(raw[:, j % RAW_SLOTS], src).then_inc(raw_in[j % RAW_SLOTS], 16)

            def expert_of(b, k):
                return sp.value_load(top_idx[0:1, bass.ds(b, 1), k], min_val=0, max_val=E - 1)

            def batch(b, with_next):
                if with_next:
                    load_x(b + 1)
                e = expert_of(b, 0)
                for j in range(RAW_SLOTS, CHUNKS):
                    load_expert(b, j, e)
                e = expert_of(b, 1)
                for j in range(CHUNKS, ECH):
                    load_expert(b, j, e)
                if with_next:
                    e = expert_of(b + 1, 0)
                    for j in range(RAW_SLOTS):
                        load_expert(b + 1, j, e)
                for hh in range(HH):
                    sp.wait_ge(out_done, HH * b + hh + 2)
                    dst = outT[bass.ds(b, 1), :, hh].rearrange("a p t -> (a p) t")
                    sp.dma_start(dst, out_sb[:, hh]).then_inc(stored, 16)

            sp.sem_inc(stored, 1)
            sp.dma_start(cond_all[:].rearrange("p b e -> p (b e)"), cond.partition_broadcast(P)).then_inc(cond_in, 16)
            for g in range(0, G, 2):
                sp.dma_start(l0_raw[:, g:g + 2], l0_w[g:g + 2].rearrange("g p w -> p g w")).then_inc(l0_in[g // 2], 16)
                if g == 2:
                    load_x(0)
                if g == 4:
                    sp.dma_start(mask[:], l0_mask).then_inc(mask_in, 16)
            sp.dma_start(bias[:], l0_bias).then_inc(bias_in, 16)
            for c in range(CHUNKS):
                if c >= RAW_SLOTS:
                    sp.wait_ge(w_lo_done, c - RAW_SLOTS + 1)
                sp.dma_start(raw[:, c % RAW_SLOTS], shared[c]).then_inc(raw_in[c % RAW_SLOTS], 16)
            sp.wait_ge(routed, ROUTED_IDX)
            e = expert_of(0, 0)
            for j in range(RAW_SLOTS):
                load_expert(0, j, e)
            with sp.Fori(0, B - 1) as b:
                batch(b, True)
            batch(B - 1, False)
            sp.wait_ge(stored, 16 * HH * B + 1)

        @block.tensor
        def _(pe):
            def first_layer(b):
                for oh in range(HH):
                    if oh == 0 and not isinstance(b, int):
                        pe.wait_ge(x1_done, HH * b)
                    pe.wait_ge(l0_hi_done, HH * b + oh + 1)
                    pe.wait_ge(x_hi_done, HH * b + HH)
                    pe.wait_ge(x_lo_done, HH * b + HH)
                    for i, (w, x) in enumerate(((l0_hi, x_hi), (l0_hi, x_lo), (l0_lo, x_hi))):
                        if w is l0_lo:
                            pe.wait_ge(l0_lo_done, HH * b + oh + 1)
                        for th in range(HH):
                            at = th * D + oh * P
                            mm = pe.matmul(l0_ps[:, oh], w[:, at:at + P], x[:, th], start=(i == 0 and th == 0), stop=(i == 2 and th == HH - 1))
                    mm.then_inc(l0_done, 1)

            def weights(s):
                if s < CHUNKS:
                    return sh_hi[:, s], sh_lo[:, s]
                return ex_hi[:, (s - CHUNKS) % RING], ex_lo[:, (s - CHUNKS) % RING]

            def gate_up(b, s):
                n = STEPS * b + s
                w_hi, w_lo = weights(s)
                if s < CHUNKS:
                    pe.wait_ge(w_lo_done, s + 1)
                else:
                    pe.wait_ge(w_lo_done, ECH * b + s + 1)
                for ps, off, free, done in ((g_ps, GATE, gelu_done, g_done), (u_ps, UP, h_done, u_done)):
                    if not isinstance(n, int) or n >= 2:
                        pe.wait_ge(free, n - 1)
                    i = 0
                    for hh in range(HH):
                        at = off + hh * P
                        for w, x in ((w_hi, x1_hi), (w_lo, x1_hi), (w_hi, x1_lo)):
                            if s == 0 and off == GATE and w is w_hi:
                                pe.wait_ge(x1_hi_done if x is x1_hi else x1_lo_done, HH * b + hh + 1)
                            mm = pe.matmul(ps[:, s % 2], w[:, at:at + P], x1_at(x, b, hh), start=(i == 0), stop=(i == 3 * HH - 1))
                            i += 1
                    mm.then_inc(done, 1)

            def down(b, s):
                n = STEPS * b + s
                w_hi, w_lo = weights(s)
                pe.wait_ge(h_lo_done, n + 1)
                if s == 0:
                    pe.wait_ge(out_done, HH * b + 1)
                for oh in range(HH):
                    at = DOWN + oh * P
                    for i, (w, x) in enumerate(((w_hi, h_hi), (w_hi, h_lo), (w_lo, h_hi))):
                        mm = pe.matmul(o_ps[:, oh], w[:, at:at + P], x[:, s % H_SLOTS], start=(s == 0 and i == 0), stop=(s == STEPS - 1 and i == 2))
                    if s == STEPS - 1 and oh == 0:
                        mm.then_inc(sum0_done, 1)
                mm.then_inc(down_done, 1)

            def batch(b, with_next):
                for s in range(STEPS):
                    if s + LAG < STEPS:
                        gate_up(b, s + LAG)
                    elif with_next:
                        gate_up(b + 1, s + LAG - STEPS)
                    down(b, s)
                    if with_next and s == L0_STEP:
                        first_layer(b + 1)

            first_layer(0)
            for s in range(LAG):
                gate_up(0, s)
            with pe.Fori(0, B - 1) as b:
                batch(b, True)
            batch(B - 1, False)

        @block.scalar
        def _(act):
            def split_x(b, hh):
                if hh == 0:
                    act.wait_ge(x_loaded, 16 * b + 16)
                    if not isinstance(b, int):
                        act.wait_ge(l0_done, HH * b)
                act.copy(x_hi[:, hh], x_in[:, hh]).then_inc(x_hi_done, 1)

            def split_l0(b, oh):
                act.wait_ge(masked, HH * b + oh + 1)
                half = lambda t: t[:].rearrange("p (h o) -> p h o", h=HH)[:, :, oh * P:(oh + 1) * P]
                act.copy(half(l0_hi), half(l0_cw)).then_inc(l0_hi_done, 1)

            def split_x1(b, hh):
                act.wait_ge(x1_done, HH * b + hh + 1)
                act.copy(x1_at(x1_hi, b, hh), x1_at(x1, b, hh)).then_inc(x1_hi_done, 1)

            def split_weights(k, dst):
                act.wait_ge(raw_in[k % RAW_SLOTS], 16 * (k // RAW_SLOTS + 1))
                act.copy(dst, raw[:, k % RAW_SLOTS]).then_inc(w_hi_done, 1)

            def step(b, s):
                n = STEPS * b + s
                act.wait_ge(g_done, n + 1)
                act.activation(gelu[:, s % 2], g_ps[:, s % 2], ACT.Gelu_apprx_tanh).then_inc(gelu_done, 1)
                j = s - SPLIT_LEAD
                if 0 <= j < ECH:
                    act.wait_ge(raw_in[j % RAW_SLOTS], (CHUNKS // RAW_SLOTS + j // RAW_SLOTS + 1 + (ECH // RAW_SLOTS) * b) * 16)
                    act.wait_ge(down_done, STEPS * b + j + 1)
                    act.copy(ex_hi[:, j % RING], raw[:, j % RAW_SLOTS]).then_inc(w_hi_done, 1)
                act.wait_ge(h_done, n + 1)
                act.copy(h_hi[:, s % H_SLOTS], h[:, s % 2]).then_inc(h_hi_done, 1)

            def batch(b, with_next):
                for s in range(STEPS):
                    step(b, s)
                    if with_next:
                        if s in (4, 5):
                            split_x(b + 1, s - 4)
                        if s in (9, 10):
                            split_l0(b + 1, s - 9)
                        if s in (L0_STEP + 2, L0_STEP + 3):
                            split_x1(b + 1, s - L0_STEP - 2)

            act.wait_ge(routed, ROUTED_SHIFTED)
            act.activation(exps[:], shifted[:], ACT.Exp).then_inc(exp_done, 1)
            for hh in range(HH):
                split_x(0, hh)
            for oh in range(HH):
                split_l0(0, oh)
            split_weights(0, sh_hi[:, 0])
            for hh in range(HH):
                split_x1(0, hh)
            for c in range(1, CHUNKS):
                split_weights(c, sh_hi[:, c])
            with act.Fori(0, B - 1) as b:
                batch(b, True)
            batch(B - 1, False)

        @block.vector
        def _(dve):
            def route_find():
                dve.wait_ge(cond_in, 16)
                for b in range(B):
                    dve.max(top[:, b], cond_all[:, b]).then_inc(routed, 1)
                for b in range(B):
                    dve.wait_ge(routed, b + 1)
                    dve.max_index(top_idx[:, b], top[:, b], cond_all[:, b]).then_inc(routed, 1)
                dve.tensor_tensor(shifted[:], top[:], top[:, :, 0:1].to_broadcast([P, B, 8]), ALU.subtract).then_inc(routed, 1)

            def route_weigh():
                r = ROUTED_SHIFTED
                dve.wait_ge(exp_done, 1)
                dve.reduce_sum(exp_sum[:], exps[:], AX_X).then_inc(routed, 1)
                dve.wait_ge(routed, r + 1)
                dve.reciprocal(exp_rsum[:], exp_sum[:]).then_inc(routed, 1)
                dve.wait_ge(routed, r + 2)
                dve.tensor_tensor(probs[:], exps[:], exp_rsum[:].unsqueeze(2).to_broadcast([P, B, 8]), ALU.mult).then_inc(routed, 1)
                dve.wait_ge(routed, r + 3)
                dve.tensor_tensor(pair_sum[:], probs[:, :, 0], probs[:, :, 1], ALU.add).then_inc(routed, 1)
                dve.wait_ge(routed, r + 4)
                dve.reciprocal(pair_rsum[:], pair_sum[:]).then_inc(routed, 1)
                dve.wait_ge(routed, r + 5)
                dve.tensor_tensor(pair[:], probs[:, :, 0:TOP_K], pair_rsum[:].unsqueeze(2).to_broadcast([P, B, TOP_K]), ALU.mult).then_inc(routed, 1)
                dve.wait_ge(routed, r + 6)
                dve.tensor_scalar(pair_rest[:], pair[:], 1.0 - SCALE, None, ALU.mult).then_inc(routed, 1)
                dve.wait_ge(routed, r + 7)
                dve.scalar_tensor_tensor(route_w[:].rearrange("p (b k) -> p b k", k=TOP_K), pair[:], SCALE, pair_rest[:],
                                         ALU.mult, ALU.add).then_inc(routed, 1)

            def pick_cond(b):
                dve.tensor_copy(cond_cur[:], cond_all[:].rearrange("p b e -> p (b e)")[:, bass.ds(b * G, G)]).then_inc(cond_picked, 1)

            def combine(b, g):
                if isinstance(b, int):
                    dve.wait_ge(l0_in[g // 2], 16)
                if g == 0:
                    dve.wait_ge(cond_picked, b + 1)
                    dve.tensor_scalar(l0_acc[:], l0_raw[:, g], cond_cur[:, g:g + 1], None, ALU.mult).then_inc(combined, 1)
                else:
                    dve.wait_ge(combined, G * b + g)
                    dve.scalar_tensor_tensor(l0_acc[:], l0_raw[:, g], cond_cur[:, g:g + 1], l0_acc[:], ALU.mult, ALU.add).then_inc(combined, 1)

            def half(t, oh):
                return t[:].rearrange("p (h o) -> p h o", h=HH)[:, :, oh * P:(oh + 1) * P]

            def apply_mask(b, oh):
                if oh == 0:
                    dve.wait_ge(combined, G * b + G)
                    if isinstance(b, int):
                        dve.wait_ge(mask_in, 16)
                dve.tensor_tensor(half(l0_cw, oh), half(l0_acc, oh), half(mask, oh), ALU.mult).then_inc(masked, 1)

            def split_l0(b, oh):
                dve.wait_ge(l0_hi_done, HH * b + oh + 1)
                dve.tensor_tensor(half(l0_lo, oh), half(l0_cw, oh), half(l0_hi, oh).bitcast(F32), ALU.subtract).then_inc(l0_lo_done, 1)

            def split_x(b, hh):
                dve.wait_ge(x_hi_done, HH * b + hh + 1)
                dve.tensor_tensor(x_lo[:, hh], x_in[:, hh], x_hi[:, hh].bitcast(F32), ALU.subtract).then_inc(x_lo_done, 1)

            def residual(b, oh):
                dve.wait_ge(l0_done, HH * b + oh + 1)
                dve.scalar_tensor_tensor(x1_at(x1, b, oh), l0_ps[:, oh], bias[:, oh:oh + 1], x_in[:, oh], ALU.add, ALU.add).then_inc(x1_done, 1)

            def split_x1(b, hh):
                dve.wait_ge(x1_hi_done, HH * b + hh + 1)
                dve.tensor_tensor(x1_at(x1_lo, b, hh), x1_at(x1, b, hh), x1_at(x1_hi, b, hh).bitcast(F32), ALU.subtract).then_inc(x1_lo_done, 1)

            def pick_route(b):
                dve.tensor_copy(route_cur[:], route_w[:, bass.ds(b * TOP_K, TOP_K)]).then_inc(route_picked, 1)

            def step(b, s):
                n = STEPS * b + s
                dve.wait_ge(gelu_done, n + 1)
                dve.wait_ge(u_done, n + 1)
                if s < CHUNKS:
                    dve.tensor_tensor(h[:, s % 2], gelu[:, s % 2], u_ps[:, s % 2], ALU.mult).then_inc(h_done, 1)
                else:
                    if s == CHUNKS:
                        dve.wait_ge(route_picked, b + 1)
                    k = s // CHUNKS - 1
                    dve.scalar_tensor_tensor(h[:, s % 2], gelu[:, s % 2], route_cur[:, k:k + 1], u_ps[:, s % 2], ALU.mult, ALU.mult).then_inc(h_done, 1)
                dve.wait_ge(h_hi_done, n + 1)
                dve.tensor_tensor(h_lo[:, s % H_SLOTS], h[:, s % 2], h_hi[:, s % H_SLOTS].bitcast(F32), ALU.subtract).then_inc(h_lo_done, 1)

            def store_ready(b):
                for hh in range(HH):
                    if hh == 0:
                        dve.wait_ge(sum0_done, b + 1)
                        dve.wait_ge(stored, 16 * HH * b + 1)
                    else:
                        dve.wait_ge(down_done, STEPS * b + STEPS)
                    dve.tensor_tensor(out_sb[:, hh], x1_at(x1, b, hh), o_ps[:, hh], ALU.add).then_inc(out_done, 1)

            def batch(b, with_next):
                for s in range(1, STEPS):
                    step(b, s)
                    if s == CHUNKS - 1:
                        pick_route(b)
                    if with_next:
                        if s == 1:
                            pick_cond(b + 1)
                            for g in range(2):
                                combine(b + 1, g)
                        if 2 <= s < G:
                            combine(b + 1, s)
                        if s == G:
                            for oh in range(HH):
                                apply_mask(b + 1, oh)
                        if s in (10, 11):
                            split_l0(b + 1, s - 10)
                            split_x(b + 1, s - 10)
                        if s in (L0_STEP + 2, L0_STEP + 3):
                            residual(b + 1, s - L0_STEP - 2)
                        if s in (L0_STEP + 4, L0_STEP + 5):
                            split_x1(b + 1, s - L0_STEP - 4)
                if with_next:
                    step(b + 1, 0)
                store_ready(b)

            dve.sem_inc(out_done, 1)
            route_find()
            pick_cond(0)
            combine(0, 0)
            combine(0, 1)
            combine(0, 2)
            route_weigh()
            for g in range(3, G):
                combine(0, g)
                if g in (5, 6):
                    split_x(0, g - 5)
            for oh in range(HH):
                apply_mask(0, oh)
            for oh in range(HH):
                split_l0(0, oh)
            dve.wait_ge(bias_in, 16)
            for oh in range(HH):
                residual(0, oh)
            for oh in range(HH):
                split_x1(0, oh)
            dve.wait_ge(routed, ROUTED_WEIGHTS)
            step(0, 0)
            with dve.Fori(0, B - 1) as b:
                batch(b, True)
            batch(B - 1, False)

        @block.gpsimd
        def _(pool):
            def split_weights(count, slot, hi, lo):
                pool.wait_ge(w_hi_done, count)
                pool.tensor_tensor(lo, raw[:, slot], hi.bitcast(F32), ALU.subtract).then_inc(w_lo_done, 1)

            for c in range(CHUNKS):
                split_weights(c + 1, c % RAW_SLOTS, sh_hi[:, c], sh_lo[:, c])
            with pool.Fori(0, B) as b:
                for j in range(ECH):
                    split_weights(ECH * b + CHUNKS + j + 1, j % RAW_SLOTS, ex_hi[:, j % RING], ex_lo[:, j % RING])


def kernel(**inputs):
    import numpy as np
    import concourse.bacc as bacc
    from concourse.bass_utils import run_bass_kernel_spmd

    def pack(gate, up, down):
        E, H, I = gate.shape
        rows = lambda a: a.reshape(E, H // P, P, I // P, P).transpose(0, 3, 2, 1, 4).reshape(E, I // P, P, H)
        return np.concatenate([rows(gate), rows(up), down.reshape(E, I // P, P, H)], axis=-1)

    a = {k: np.asarray(v) for k, v in inputs.items()}
    B, T, D = a["x"].shape
    G = a["L0_cond_weight"].shape[0]
    HH = D // P
    arrays = {
        "xT": a["x"].transpose(0, 2, 1).reshape(B, HH, P, T).transpose(0, 2, 1, 3),
        "cond": a["cond_8"].reshape(-1),
        "l0_w": a["L0_cond_weight"].transpose(0, 2, 1).reshape(G, HH, P, D).transpose(0, 2, 1, 3).reshape(G, P, HH * D),
        "l0_mask": a["L0_cond_mask"].T.reshape(HH, P, D).transpose(1, 0, 2).reshape(P, HH * D),
        "l0_bias": a["L0_cond_bias"].reshape(HH, P).T,
        "experts": pack(a["L1_cond_skill_gate"], a["L1_cond_skill_up"], a["L1_cond_skill_down"]),
        "shared": pack(a["L1_cond_shared_gate"][None], a["L1_cond_shared_up"][None], a["L1_cond_shared_down"][None])[0],
    }
    arrays = {k: np.ascontiguousarray(v) for k, v in arrays.items()}
    nc = bacc.Bacc("TRN2", target_bir_lowering=False, num_devices=1)
    args = [nc.dram_tensor(k, v.shape, mybir.dt.from_np(v.dtype), kind="ExternalInput").ap() for k, v in arrays.items()]
    outT = nc.dram_tensor("outT", (B, P, HH, T), F32, kind="ExternalOutput").ap()
    build(nc, *args, outT)
    r = run_bass_kernel_spmd(nc, [arrays], core_ids=[0])
    out = r.results[0]["outT"]
    return np.ascontiguousarray(out.transpose(0, 3, 2, 1).reshape(B, T, D))
```

```python
from contextlib import ExitStack

import concourse.bass as bass
from concourse import mybir

P = 128
F32 = mybir.dt.float32
F32R = mybir.dt.float32r
U32 = mybir.dt.uint32
ALU = mybir.AluOpType
ACT = mybir.ActivationFunctionType
AX_X = mybir.AxisListType.X

TOP_K = 2
SCALE = 1.0 / 12
LAG = 2
ACT_SHARED = 4
RAW_SLOTS = 8
RING = 8
H_SLOTS = LAG + 1
SPLIT_LEAD = 4
WARM_UP = 34
L0_STEP = 13


def build(nc, xT, cond, l0_w, l0_mask, l0_bias, experts, shared, outT):
    B, _, HH, T = xT.shape
    G = l0_w.shape[0]
    E, CHUNKS, _, WC = experts.shape
    D = HH * P
    L0C = HH * D
    GATE, UP, DOWN = 0, D, 2 * D
    STEPS = (1 + TOP_K) * CHUNKS
    ECH = TOP_K * CHUNKS

    OUT_PIECES = [(hh, slice(0, T)) for hh in range(HH - 1)] + [(HH - 1, slice(t, t + T // 2)) for t in (0, T // 2)]
    ROUTED_IDX = 2 * B
    ROUTED_SHIFTED = ROUTED_IDX + 1
    ROUTED_WEIGHTS = ROUTED_SHIFTED + 8

    assert RAW_SLOTS == CHUNKS == RING and STEPS % 2 == 0 and STEPS % H_SLOTS == 0 and G == E == 8

    with ExitStack() as ctx:
        def sb(name, shape, dt=F32):
            return ctx.enter_context(nc.sbuf_tensor(name, shape, dt))

        def psum(name, shape):
            return ctx.enter_context(nc.psum_tensor(name, shape, F32))

        def sem(name):
            return ctx.enter_context(nc.semaphore(name))

        cond_all = sb("cond_all", [P, B, E])
        top = sb("top", [P, B, 8])
        top_idx = sb("top_idx", [P, B, 8], U32)
        shifted = sb("shifted", [P, B, 8])
        exps = sb("exps", [P, B, 8])
        exp_sum = sb("exp_sum", [P, B])
        exp_rsum = sb("exp_rsum", [P, B])
        probs = sb("probs", [P, B, 8])
        pair_sum = sb("pair_sum", [P, B])
        pair_rsum = sb("pair_rsum", [P, B])
        pair = sb("pair", [P, B, TOP_K])
        pair_rest = sb("pair_rest", [P, B, TOP_K])
        route_w = sb("route_w", [P, B * TOP_K])
        cond_cur = sb("cond_cur", [P, G])
        route_cur = sb("route_cur", [P, TOP_K])
        l0_raw = sb("l0_raw", [P, G, L0C])
        mask = sb("mask", [P, L0C])
        bias = sb("bias", [P, HH])
        l0_acc = sb("l0_acc", [P, L0C])
        l0_hi = sb("l0_hi", [P, L0C], F32R)
        l0_lo = sb("l0_lo", [P, L0C], F32R)
        x_in = sb("x_in", [P, HH, T])
        x_hi = sb("x_hi", [P, HH, T], F32R)
        x_lo = sb("x_lo", [P, HH, T], F32R)
        x1 = sb("x1", [P, 2 * HH * T])
        x1_hi = sb("x1_hi", [P, 2 * HH * T], F32R)
        x1_lo = sb("x1_lo", [P, 2 * HH * T], F32R)
        raw = sb("raw", [P, RAW_SLOTS, WC])
        sh_hi = sb("sh_hi", [P, CHUNKS, WC], F32R)
        sh_lo = sb("sh_lo", [P, CHUNKS, WC], F32R)
        ex_hi = sb("ex_hi", [P, RING, WC], F32R)
        ex_lo = sb("ex_lo", [P, RING, WC], F32R)
        gelu = sb("gelu", [P, 2, T])
        h = sb("h", [P, 2, T])
        h_hi = sb("h_hi", [P, H_SLOTS, T], F32R)
        h_lo = sb("h_lo", [P, H_SLOTS, T], F32R)
        out_sb = sb("out_sb", [P, HH, T])
        zeros = sb("zeros", [P, T], F32R)

        g_ps = psum("g_ps", [P, 2, T])
        u_ps = psum("u_ps", [P, 2, T])
        o_ps = psum("o_ps", [P, HH, T])
        l0_ps = psum("l0_ps", [P, HH, T])

        zeroed = sem("zeroed")
        cond_in = sem("cond_in")
        l0_in = [sem(f"l0_in{g}") for g in range(G // 2)]
        mask_in = sem("mask_in")
        bias_in = sem("bias_in")
        x_loaded = [sem(f"x_loaded{hh}") for hh in range(HH)]
        raw_in = [sem(f"raw_in{i}") for i in range(RAW_SLOTS)]
        routed = sem("routed")
        exp_done = sem("exp_done")
        cond_picked = sem("cond_picked")
        route_picked = sem("route_picked")
        combined = sem("combined")
        masked = sem("masked")
        l0_hi_done = sem("l0_hi_done")
        l0_lo_done = sem("l0_lo_done")
        x_hi_done = sem("x_hi_done")
        x_lo_done = sem("x_lo_done")
        l0_done = sem("l0_done")
        x1_done = sem("x1_done")
        x1_hi_done = sem("x1_hi_done")
        x1_lo_done = sem("x1_lo_done")
        w_hi_done = sem("w_hi_done")
        sh_hi_done = sem("sh_hi_done")
        w_lo_done = sem("w_lo_done")
        g_done = sem("g_done")
        u_done = sem("u_done")
        gelu_done = sem("gelu_done")
        h_done = sem("h_done")
        h_hi_done = sem("h_hi_done")
        h_lo_done = sem("h_lo_done")
        down_done = sem("down_done")
        sum0_done = sem("sum0_done")
        out_done = sem("out_done")
        stored = sem("stored")

        def x1_at(t, b, hh):
            at = (b % 2) * (HH * T) + hh * T
            return t[:, bass.ds(at, T)]

        block = ctx.enter_context(nc.Block())

        @block.sync
        def _(sp):
            def load_x(b):
                if not isinstance(b, int):
                    sp.wait_ge(x1_done, HH * b)
                for hh in range(HH):
                    sp.dma_start(x_in[:, hh], xT[bass.ds(b, 1), :, hh].rearrange("a p t -> (a p) t")).then_inc(x_loaded[hh], 16)

            def load_expert(b, j, e):
                sp.wait_ge(w_lo_done, ECH * b + CHUNKS + j - RAW_SLOTS + 1)
                src = experts[bass.ds(e, 1), j % CHUNKS].rearrange("a p w -> (a p) w")
                sp.dma_start(raw[:, j % RAW_SLOTS], src).then_inc(raw_in[j % RAW_SLOTS], 16)

            def expert_of(b, k):
                return sp.value_load(top_idx[0:1, bass.ds(b, 1), k], min_val=0, max_val=E - 1)

            def batch(b, with_next):
                if with_next:
                    load_x(b + 1)
                e = expert_of(b, 1)
                for j in range(CHUNKS, ECH):
                    load_expert(b, j, e)
                if with_next:
                    e = expert_of(b + 1, 0)
                    for j in range(CHUNKS):
                        load_expert(b + 1, j, e)
                for i, (hh, tokens) in enumerate(OUT_PIECES):
                    sp.wait_ge(out_done, len(OUT_PIECES) * b + i + 2)
                    dst = outT[bass.ds(b, 1), :, hh, tokens].rearrange("a p t -> (a p) t")
                    sp.dma_start(dst, out_sb[:, hh, tokens]).then_inc(stored, 16)

            sp.sem_inc(stored, 1)
            sp.dma_start(cond_all[:].rearrange("p b e -> p (b e)"), cond.partition_broadcast(P)).then_inc(cond_in, 16)
            for g in range(0, G, 2):
                sp.dma_start(l0_raw[:, g:g + 2], l0_w[g:g + 2].rearrange("g p w -> p g w")).then_inc(l0_in[g // 2], 16)
            sp.dma_start(mask[:], l0_mask).then_inc(mask_in, 16)
            load_x(0)
            sp.dma_start(bias[:], l0_bias).then_inc(bias_in, 16)
            for c in range(CHUNKS):
                sp.dma_start(raw[:, c % RAW_SLOTS], shared[c]).then_inc(raw_in[c % RAW_SLOTS], 16)
            sp.wait_ge(routed, ROUTED_IDX)
            e = expert_of(0, 0)
            for j in range(CHUNKS):
                load_expert(0, j, e)
            with sp.Fori(0, B - 1) as b:
                batch(b, True)
            batch(B - 1, False)
            sp.wait_ge(stored, 16 * len(OUT_PIECES) * B + 1)

        @block.tensor
        def _(pe):
            def first_layer(b):
                if not isinstance(b, int):
                    pe.wait_ge(x1_done, HH * b)
                for oh in range(HH):
                    for th in range(HH):
                        for w, w_done in ((l0_hi, l0_hi_done), (l0_lo, l0_lo_done)):
                            if th == 0:
                                pe.wait_ge(w_done, HH * b + oh + 1)
                            if oh == 0 and w is l0_hi:
                                pe.wait_ge(x_hi_done, HH * b + th + 1)
                            at = oh * D + th * P
                            pe.matmul(l0_ps[:, oh], w[:, at:at + P], x_hi[:, th], start=(th == 0 and w is l0_hi), stop=False)
                pe.wait_ge(x_lo_done, HH * b + HH)
                for oh in range(HH):
                    for th in range(HH):
                        at = oh * D + th * P
                        mm = pe.matmul(l0_ps[:, oh], l0_hi[:, at:at + P], x_lo[:, th], start=False, stop=(th == HH - 1))
                    mm.then_inc(l0_done, 1)

            def weights(s):
                if s < CHUNKS:
                    return sh_hi[:, s], sh_lo[:, s]
                return ex_hi[:, (s - CHUNKS) % RING], ex_lo[:, (s - CHUNKS) % RING]

            def gate_up(b, s):
                n = STEPS * b + s
                w_hi, w_lo = weights(s)
                if s < CHUNKS:
                    pe.wait_ge(w_lo_done, s + 1)
                else:
                    pe.wait_ge(w_lo_done, ECH * b + s + 1)
                gate, up = (g_ps[:, s % 2], GATE), (u_ps[:, s % 2], UP)
                for hh in range(HH):
                    if s == 0:
                        pe.wait_ge(x1_hi_done, HH * b + hh + 1)
                    for (ps, off), free in ((gate, gelu_done), (up, h_done)):
                        if hh == 0 and (not isinstance(n, int) or n >= 2):
                            pe.wait_ge(free, n - 1)
                        at = off + hh * P
                        for w in (w_hi, w_lo):
                            pe.matmul(ps, w[:, at:at + P], x1_at(x1_hi, b, hh), start=(hh == 0 and w is w_hi), stop=False)
                for (ps, off), done in ((gate, g_done), (up, u_done)):
                    for hh in range(HH):
                        if s == 0 and off == GATE:
                            pe.wait_ge(x1_lo_done, HH * b + hh + 1)
                        at = off + hh * P
                        mm = pe.matmul(ps, w_hi[:, at:at + P], x1_at(x1_lo, b, hh), start=False, stop=(hh == HH - 1))
                    mm.then_inc(done, 1)

            def down(b, s):
                n = STEPS * b + s
                w_hi, w_lo = weights(s)
                pe.wait_ge(h_lo_done, n + 1)
                if s == 0:
                    pe.wait_ge(out_done, len(OUT_PIECES) * b + 1)
                for oh in range(HH):
                    at = DOWN + oh * P
                    for i, (w, x) in enumerate(((w_hi, h_hi), (w_hi, h_lo), (w_lo, h_hi))):
                        mm = pe.matmul(o_ps[:, oh], w[:, at:at + P], x[:, s % H_SLOTS], start=(s == 0 and i == 0), stop=(s == STEPS - 1 and i == 2))
                    if s == STEPS - 1 and oh == 0:
                        mm.then_inc(sum0_done, 1)
                mm.then_inc(down_done, 1)

            def batch(b, with_next):
                for s in range(STEPS):
                    if s + LAG < STEPS:
                        gate_up(b, s + LAG)
                    elif with_next:
                        gate_up(b + 1, s + LAG - STEPS)
                    down(b, s)
                    if with_next and s == L0_STEP:
                        first_layer(b + 1)

            pe.wait_ge(zeroed, 1)
            for _ in range(WARM_UP):
                pe.matmul(l0_ps[:, HH - 1], zeros[:, 0:P], zeros[:], start=True, stop=True)
            first_layer(0)
            for s in range(LAG):
                gate_up(0, s)
            with pe.Fori(0, B - 1) as b:
                batch(b, True)
            batch(B - 1, False)

        @block.scalar
        def _(act):
            def split_x(b, hh):
                act.wait_ge(x_loaded[hh], 16 * b + 16)
                if hh == 0 and not isinstance(b, int):
                    act.wait_ge(l0_done, HH * b)
                act.copy(x_hi[:, hh], x_in[:, hh]).then_inc(x_hi_done, 1)

            def split_l0(b, oh):
                act.wait_ge(masked, HH * b + oh + 1)
                act.copy(l0_hi[:, oh * D:(oh + 1) * D], l0_acc[:, oh * D:(oh + 1) * D]).then_inc(l0_hi_done, 1)

            def split_x1(b, hh):
                act.wait_ge(x1_done, HH * b + hh + 1)
                act.copy(x1_at(x1_hi, b, hh), x1_at(x1, b, hh)).then_inc(x1_hi_done, 1)

            def split_weights(k, dst):
                act.wait_ge(raw_in[k % RAW_SLOTS], 16 * (k // RAW_SLOTS + 1))
                act.copy(dst, raw[:, k % RAW_SLOTS]).then_inc(w_hi_done, 1)

            def step(b, s):
                n = STEPS * b + s
                act.wait_ge(g_done, n + 1)
                act.activation(gelu[:, s % 2], g_ps[:, s % 2], ACT.Gelu_apprx_tanh).then_inc(gelu_done, 1)
                j = s - SPLIT_LEAD
                if 0 <= j < ECH:
                    act.wait_ge(raw_in[j % RAW_SLOTS], (CHUNKS // RAW_SLOTS + j // RAW_SLOTS + 1 + (ECH // RAW_SLOTS) * b) * 16)
                    act.wait_ge(down_done, STEPS * b + j + 1)
                    act.copy(ex_hi[:, j % RING], raw[:, j % RAW_SLOTS]).then_inc(w_hi_done, 1)
                act.wait_ge(h_done, n + 1)
                act.copy(h_hi[:, s % H_SLOTS], h[:, s % 2]).then_inc(h_hi_done, 1)

            def batch(b, with_next):
                for s in range(STEPS):
                    step(b, s)
                    if with_next:
                        if s in (4, 5):
                            split_x(b + 1, s - 4)
                        if s in (9, 10):
                            split_l0(b + 1, s - 9)
                        if s in (L0_STEP + 2, L0_STEP + 3):
                            split_x1(b + 1, s - L0_STEP - 2)

            act.wait_ge(routed, ROUTED_SHIFTED)
            act.activation(exps[:], shifted[:], ACT.Exp).then_inc(exp_done, 1)
            act.activation(gelu[:, 0, 0:8], shifted[:, 0], ACT.Gelu_apprx_tanh)
            for hh in range(HH):
                split_x(0, hh)
                split_l0(0, hh)
            for c in range(ACT_SHARED):
                split_weights(c, sh_hi[:, c])
                if c < HH:
                    split_x1(0, c)
            with act.Fori(0, B - 1) as b:
                batch(b, True)
            batch(B - 1, False)

        @block.vector
        def _(dve):
            def route_find():
                dve.wait_ge(cond_in, 16)
                for b in range(B):
                    dve.max(top[:, b], cond_all[:, b]).then_inc(routed, 1)
                for b in range(B):
                    dve.wait_ge(routed, b + 1)
                    dve.max_index(top_idx[:, b], top[:, b], cond_all[:, b]).then_inc(routed, 1)
                dve.tensor_tensor(shifted[:], top[:], top[:, :, 0:1].to_broadcast([P, B, 8]), ALU.subtract).then_inc(routed, 1)

            def route_weigh():
                r = ROUTED_SHIFTED
                dve.wait_ge(exp_done, 1)
                dve.reduce_sum(exp_sum[:], exps[:], AX_X).then_inc(routed, 1)
                dve.wait_ge(routed, r + 1)
                dve.reciprocal(exp_rsum[:], exp_sum[:]).then_inc(routed, 1)
                dve.wait_ge(routed, r + 2)
                dve.tensor_tensor(probs[:], exps[:], exp_rsum[:].unsqueeze(2).to_broadcast([P, B, 8]), ALU.mult).then_inc(routed, 1)
                dve.wait_ge(routed, r + 3)
                dve.tensor_tensor(pair_sum[:], probs[:, :, 0], probs[:, :, 1], ALU.add).then_inc(routed, 1)
                dve.wait_ge(routed, r + 4)
                dve.reciprocal(pair_rsum[:], pair_sum[:]).then_inc(routed, 1)
                dve.wait_ge(routed, r + 5)
                dve.tensor_tensor(pair[:], probs[:, :, 0:TOP_K], pair_rsum[:].unsqueeze(2).to_broadcast([P, B, TOP_K]), ALU.mult).then_inc(routed, 1)
                dve.wait_ge(routed, r + 6)
                dve.tensor_scalar(pair_rest[:], pair[:], 1.0 - SCALE, None, ALU.mult).then_inc(routed, 1)
                dve.wait_ge(routed, r + 7)
                dve.scalar_tensor_tensor(route_w[:].rearrange("p (b k) -> p b k", k=TOP_K), pair[:], SCALE, pair_rest[:],
                                         ALU.mult, ALU.add).then_inc(routed, 1)

            def pick_cond(b):
                dve.tensor_copy(cond_cur[:], cond_all[:].rearrange("p b e -> p (b e)")[:, bass.ds(b * G, G)]).then_inc(cond_picked, 1)

            def combine(b, g):
                if isinstance(b, int):
                    dve.wait_ge(l0_in[g // 2], 16)
                if g == 0:
                    dve.wait_ge(cond_picked, b + 1)
                for oh in range(HH):
                    acc, w = half(l0_acc, oh), l0_raw[:, g, oh * D:(oh + 1) * D]
                    if g == 0:
                        dve.tensor_scalar(acc, w, cond_cur[:, g:g + 1], None, ALU.mult).then_inc(combined, 1)
                    else:
                        dve.wait_ge(combined, HH * (G * b + g - 1) + oh + 1)
                        dve.scalar_tensor_tensor(acc, w, cond_cur[:, g:g + 1], acc, ALU.mult, ALU.add).then_inc(combined, 1)

            def half(t, oh):
                return t[:, oh * D:(oh + 1) * D]

            def apply_mask(b, oh):
                dve.wait_ge(combined, HH * (G * b + G - 1) + oh + 1)
                if isinstance(b, int):
                    dve.wait_ge(mask_in, 16)
                dve.tensor_tensor(half(l0_acc, oh), half(l0_acc, oh), half(mask, oh), ALU.mult).then_inc(masked, 1)

            def split_l0(b, oh):
                dve.wait_ge(l0_hi_done, HH * b + oh + 1)
                dve.tensor_tensor(half(l0_lo, oh), half(l0_acc, oh), half(l0_hi, oh).bitcast(F32), ALU.subtract).then_inc(l0_lo_done, 1)

            def split_x(b, hh):
                dve.wait_ge(x_hi_done, HH * b + hh + 1)
                dve.tensor_tensor(x_lo[:, hh], x_in[:, hh], x_hi[:, hh].bitcast(F32), ALU.subtract).then_inc(x_lo_done, 1)

            def residual(b, oh):
                dve.wait_ge(l0_done, HH * b + oh + 1)
                dve.scalar_tensor_tensor(x1_at(x1, b, oh), l0_ps[:, oh], bias[:, oh:oh + 1], x_in[:, oh], ALU.add, ALU.add).then_inc(x1_done, 1)

            def split_x1(b, hh):
                dve.wait_ge(x1_hi_done, HH * b + hh + 1)
                dve.tensor_tensor(x1_at(x1_lo, b, hh), x1_at(x1, b, hh), x1_at(x1_hi, b, hh).bitcast(F32), ALU.subtract).then_inc(x1_lo_done, 1)

            def pick_route(b):
                dve.tensor_copy(route_cur[:], route_w[:, bass.ds(b * TOP_K, TOP_K)]).then_inc(route_picked, 1)

            def step(b, s):
                n = STEPS * b + s
                dve.wait_ge(gelu_done, n + 1)
                dve.wait_ge(u_done, n + 1)
                if s < CHUNKS:
                    dve.tensor_tensor(h[:, s % 2], gelu[:, s % 2], u_ps[:, s % 2], ALU.mult).then_inc(h_done, 1)
                else:
                    if s == CHUNKS:
                        dve.wait_ge(route_picked, b + 1)
                    k = s // CHUNKS - 1
                    dve.scalar_tensor_tensor(h[:, s % 2], gelu[:, s % 2], route_cur[:, k:k + 1], u_ps[:, s % 2], ALU.mult, ALU.mult).then_inc(h_done, 1)
                dve.wait_ge(h_hi_done, n + 1)
                dve.tensor_tensor(h_lo[:, s % H_SLOTS], h[:, s % 2], h_hi[:, s % H_SLOTS].bitcast(F32), ALU.subtract).then_inc(h_lo_done, 1)

            def store_ready(b):
                dve.wait_ge(stored, 16 * len(OUT_PIECES) * b + 1)
                dve.wait_ge(sum0_done, b + 1)
                for i, (hh, tokens) in enumerate(OUT_PIECES):
                    if i == HH - 1:
                        dve.wait_ge(down_done, STEPS * b + STEPS)
                    x1_piece = x1[:, bass.ds((b % 2) * (HH * T) + hh * T + tokens.start, tokens.stop - tokens.start)]
                    dve.tensor_tensor(out_sb[:, hh, tokens], x1_piece, o_ps[:, hh, tokens], ALU.add).then_inc(out_done, 1)

            def batch(b, with_next):
                for s in range(1, STEPS):
                    step(b, s)
                    if s == CHUNKS - 1:
                        pick_route(b)
                    if with_next:
                        if s == 1:
                            pick_cond(b + 1)
                            for g in range(2):
                                combine(b + 1, g)
                        if 2 <= s < G:
                            combine(b + 1, s)
                        if s == G:
                            for oh in range(HH):
                                apply_mask(b + 1, oh)
                        if s in (10, 11):
                            split_l0(b + 1, s - 10)
                            split_x(b + 1, s - 10)
                        if s in (L0_STEP + 2, L0_STEP + 3):
                            residual(b + 1, s - L0_STEP - 2)
                        if s in (L0_STEP + 4, L0_STEP + 5):
                            split_x1(b + 1, s - L0_STEP - 4)
                if with_next:
                    step(b + 1, 0)
                store_ready(b)

            dve.sem_inc(out_done, 1)
            route_find()
            pick_cond(0)
            for g in range(G):
                combine(0, g)
            for oh in range(HH):
                apply_mask(0, oh)
            for oh in range(HH):
                split_l0(0, oh)
            split_x(0, 1)
            dve.wait_ge(bias_in, 16)
            for oh in range(HH):
                residual(0, oh)
            for oh in range(HH):
                split_x1(0, oh)
            route_weigh()
            for c in range(ACT_SHARED, CHUNKS):
                dve.wait_ge(raw_in[c], 16)
                dve.tensor_copy(sh_hi[:, c], raw[:, c]).then_inc(sh_hi_done, 1)
            dve.wait_ge(routed, ROUTED_WEIGHTS)
            step(0, 0)
            with dve.Fori(0, B - 1) as b:
                batch(b, True)
            batch(B - 1, False)

        @block.gpsimd
        def _(pool):
            def split_weights(hi_done, count, slot, hi, lo):
                pool.wait_ge(hi_done, count)
                pool.tensor_tensor(lo, raw[:, slot], hi.bitcast(F32), ALU.subtract).then_inc(w_lo_done, 1)

            pool.memset(zeros[:].bitcast(U32), 0).then_inc(zeroed, 1)
            pool.wait_ge(x_hi_done, 1)
            pool.tensor_tensor(x_lo[:, 0], x_in[:, 0], x_hi[:, 0].bitcast(F32), ALU.subtract).then_inc(x_lo_done, 1)
            for c in range(CHUNKS):
                if c < ACT_SHARED:
                    split_weights(w_hi_done, c + 1, c, sh_hi[:, c], sh_lo[:, c])
                else:
                    split_weights(sh_hi_done, c - ACT_SHARED + 1, c, sh_hi[:, c], sh_lo[:, c])
            with pool.Fori(0, B) as b:
                for j in range(ECH):
                    split_weights(w_hi_done, ECH * b + ACT_SHARED + j + 1, j % RAW_SLOTS, ex_hi[:, j % RING], ex_lo[:, j % RING])

def kernel(**inputs):
    import numpy as np
    import concourse.bacc as bacc
    from concourse.bass_utils import run_bass_kernel_spmd

    def pack(gate, up, down):
        E, H, I = gate.shape
        rows = lambda a: a.reshape(E, H // P, P, I // P, P).transpose(0, 3, 2, 1, 4).reshape(E, I // P, P, H)
        return np.concatenate([rows(gate), rows(up), down.reshape(E, I // P, P, H)], axis=-1)

    def by_halves(w):
        w = w.reshape(*w.shape[:-2], HH, P, HH, P)
        return np.moveaxis(w, (-1, -4, -2, -3), (-4, -3, -2, -1)).reshape(*w.shape[:-4], P, HH * D)

    a = {k: np.asarray(v) for k, v in inputs.items()}
    B, T, D = a["x"].shape
    G = a["L0_cond_weight"].shape[0]
    HH = D // P
    arrays = {
        "xT": a["x"].transpose(0, 2, 1).reshape(B, HH, P, T).transpose(0, 2, 1, 3),
        "cond": a["cond_8"].reshape(-1),
        "l0_w": by_halves(a["L0_cond_weight"]),
        "l0_mask": by_halves(a["L0_cond_mask"]),
        "l0_bias": a["L0_cond_bias"].reshape(HH, P).T,
        "experts": pack(a["L1_cond_skill_gate"], a["L1_cond_skill_up"], a["L1_cond_skill_down"]),
        "shared": pack(a["L1_cond_shared_gate"][None], a["L1_cond_shared_up"][None], a["L1_cond_shared_down"][None])[0],
    }
    arrays = {k: np.ascontiguousarray(v) for k, v in arrays.items()}
    nc = bacc.Bacc("TRN2", target_bir_lowering=False, num_devices=1)
    args = [nc.dram_tensor(k, v.shape, mybir.dt.from_np(v.dtype), kind="ExternalInput").ap() for k, v in arrays.items()]
    outT = nc.dram_tensor("outT", (B, P, HH, T), F32, kind="ExternalOutput").ap()
    build(nc, *args, outT)
    r = run_bass_kernel_spmd(nc, [arrays], core_ids=[0])
    out = r.results[0]["outT"]
    return np.ascontiguousarray(out.transpose(0, 3, 2, 1).reshape(B, T, D))
```
